# Optimizing a Trainium2 kernel written in Bass

```python
import numpy as np
import jax
import jax.numpy as jnp

def _softmax(x, axis=-1):
    return jax.nn.softmax(x, axis=axis)

def _gelu(x):
    return jax.nn.gelu(x, approximate=True)

def _silu(x):
    return jax.nn.silu(x)

def _sigmoid(x):
    return jax.nn.sigmoid(x)

def _layernorm(x, axis=-1, eps=1e-05):
    m = jnp.mean(x, axis=axis, keepdims=True)
    v = jnp.var(x, axis=axis, keepdims=True)
    return (x - m) / jnp.sqrt(v + eps)

def _scatter_add(tgt, idx, src, axis=0):
    return tgt.at[idx].add(src)

def _segment_sum(src, seg, n):
    return jax.ops.segment_sum(src, seg, n)
kernel_name = 'mk_xattn_seq_d1_seqx_r4_a8b0ba'

def setup_inputs(seed: int=0):
    np.random.seed(seed)
    _w = jnp.asarray

    def _rec_inputs():
        import jax
        import jax.numpy as jnp
        _rk = jax.random.key(seed)
        x = -0.0003929 + 0.9999 * jax.random.normal(jax.random.fold_in(_rk, 1), (1, 2048, 256), jnp.float32)
        _lenS = 2048 - jax.random.randint(jax.random.fold_in(_rk, 7), (1,), 0, max(1, 2048 // 4) + 1, jnp.int32)
        _lenS2 = 1601 - jax.random.randint(jax.random.fold_in(_rk, 8), (1,), 0, max(1, 1601 // 4) + 1, jnp.int32)
        _ctx_1024P = jax.random.normal(jax.random.fold_in(_rk, 11), (1, 16, 256), jnp.float32)
        _ctx_1024c = jax.random.dirichlet(jax.random.fold_in(_rk, 511), 0.3 * jnp.ones((16,), jnp.float32), (1, 1601))
        _ctx_1024t = jnp.einsum('bsk,bkd->bsd', _ctx_1024c, _ctx_1024P)
        _ctx_1024t = _ctx_1024t * jax.lax.rsqrt(jnp.mean(jnp.square(_ctx_1024t)) + 1e-12) * 0.953939
        ctx_1024 = 0.000227908 + 0.99994 * (_ctx_1024t + 0.3 * jax.random.normal(jax.random.fold_in(_rk, 611), (1, 1601, 256), jnp.float32))
        itok_BxS_0_255 = jax.random.randint(jax.random.fold_in(_rk, 12), (1, 2048), 0, 64, jnp.int32)
        return (x, ctx_1024, itok_BxS_0_255)
    x, ctx_1024, itok_BxS_0_255 = _rec_inputs()

    def _L0_xattn_setup():
        import jax, jax.numpy as jnp
        import numpy as np
        import math
        EPS_RMS = 1.1920929e-07
        EPS_DEN = 1e-06

        def rmsnorm(x, gamma):
            ms = jnp.mean(x * x, axis=-1, keepdims=True)
            return x * jax.lax.rsqrt(ms + EPS_RMS) * gamma
        key = jax.random.key(seed)
        ks = jax.random.split(key, 8)
        B, T, K, D = (4, 1024, 64, 256)
        x_tokens = jax.random.normal(ks[0], (B, T, D), dtype=jnp.float32)
        ctx = jax.random.normal(ks[1], (B, K, D), dtype=jnp.float32)
        idx = jnp.sort(jax.random.randint(ks[2], (B, T), 0, K), axis=-1)
        s = 1.0 / math.sqrt(D)
        Wq = jax.random.normal(ks[3], (D, D), dtype=jnp.float32) * s
        Wk = jax.random.normal(ks[4], (D, D), dtype=jnp.float32) * s
        Wv = jax.random.normal(ks[5], (D, D), dtype=jnp.float32) * s
        Wo = jax.random.normal(ks[6], (D, D), dtype=jnp.float32) * s
        return {'x_tokens': x_tokens, 'ctx': ctx, 'ctx_index_per_token': idx, 'gamma_q': jnp.ones((D,), jnp.float32), 'gamma_kv': jnp.ones((D,), jnp.float32), 'Wq': Wq, 'Wk': Wk, 'Wv': Wv, 'Wo': Wo}
    _L0_xattn_all = _L0_xattn_setup()
    _L0_xattn_in = {k: v for k, v in _L0_xattn_all.items() if k in ('gamma_q', 'gamma_kv', 'Wq', 'Wk', 'Wv', 'Wo')}
    del _L0_xattn_all
    return {'x': x, 'ctx_1024': ctx_1024, 'itok_BxS_0_255': itok_BxS_0_255, 'L0_xattn_gamma_q': _L0_xattn_in['gamma_q'], 'L0_xattn_gamma_kv': _L0_xattn_in['gamma_kv'], 'L0_xattn_Wq': _L0_xattn_in['Wq'], 'L0_xattn_Wk': _L0_xattn_in['Wk'], 'L0_xattn_Wv': _L0_xattn_in['Wv'], 'L0_xattn_Wo': _L0_xattn_in['Wo']}

def reference(x, ctx_1024, itok_BxS_0_255, L0_xattn_gamma_q, L0_xattn_gamma_kv, L0_xattn_Wq, L0_xattn_Wk, L0_xattn_Wv, L0_xattn_Wo):
    import jax
    import jax.numpy as jnp

    def _L0_xattn_ref(x_tokens, ctx, ctx_index_per_token, gamma_q, gamma_kv, Wq, Wk, Wv, Wo):
        import jax, jax.numpy as jnp
        import numpy as np
        import math
        EPS_RMS = 1.1920929e-07
        EPS_DEN = 1e-06

        def rmsnorm(x, gamma):
            ms = jnp.mean(x * x, axis=-1, keepdims=True)
            return x * jax.lax.rsqrt(ms + EPS_RMS) * gamma
        B, T, D = x_tokens.shape
        K = ctx.shape[1]
        H = 16
        hd = D // H

        def split(x):
            return x.reshape(B, -1, H, hd).transpose(0, 2, 1, 3)
        q = split(rmsnorm(x_tokens, gamma_q) @ Wq.T)
        kn = rmsnorm(ctx, gamma_kv)
        k = split(kn @ Wk.T)
        v = split(kn @ Wv.T)
        ctx_pos = jnp.arange(K)[None, None, :]
        mask = (jnp.abs(ctx_pos - ctx_index_per_token[:, :, None]) <= 1)[:, None]
        scores = jnp.einsum('bhqd,bhkd->bhqk', q, k) / math.sqrt(hd)
        w = jnp.square(jax.nn.relu(scores))
        w = jnp.where(mask, w, 0.0)
        denom = jnp.maximum(w.sum(-1, keepdims=True), EPS_DEN)
        out = jnp.einsum('bhqk,bhkd->bhqd', w / denom, v)
        out = out.transpose(0, 2, 1, 3).reshape(B, T, D)
        return x_tokens + out @ Wo.T
    x = _L0_xattn_ref(x, ctx_1024, itok_BxS_0_255, L0_xattn_gamma_q, L0_xattn_gamma_kv, L0_xattn_Wq, L0_xattn_Wk, L0_xattn_Wv, L0_xattn_Wo)
    return x

_drawn_inputs = setup_inputs


def setup_inputs(seed=0):
    import zlib

    import numpy as np

    out = dict(_drawn_inputs(seed))
    spreads = {'L0_xattn_gamma_q': (1.0, 0.2), 'L0_xattn_gamma_kv': (1.0, 0.2)}
    factors = {}
    for name, (base, spread) in spreads.items():
        noise = np.random.default_rng([zlib.crc32(name.encode()), seed]).standard_normal(out[name].shape)
        drawn = base * np.exp(spread * noise) if base else spread * noise
        out[name] = jnp.asarray(drawn.astype(out[name].dtype))
    for name, factor in factors.items():
        out[name] = (out[name] * factor).astype(out[name].dtype)
    return out
```

```python
from contextlib import ExitStack

import numpy as np

import concourse.bass as bass
from concourse import mybir

F32 = mybir.dt.float32
F32R = mybir.dt.float32r
I32 = mybir.dt.int32
ALU = mybir.AluOpType
ACT = mybir.ActivationFunctionType
AX_X = mybir.AxisListType.X

P = 128
EPS_RMS = 1.1920929e-07
EPS_DEN = 1e-06
HEADS = 16
NEIGHBOURS = 3


def local_attention(nc, x, x_t, ctx, ctx_t, index_row, index_cols, gamma_q, gamma_kv, wq_t, wkv_t, wo_t, y):
    T, D = x.shape
    HD = D // HEADS
    C = D // P
    BLOCKS = ctx.shape[0] // P
    PAIR = 2 * P
    PAIRS = T // PAIR
    LAST = PAIRS - 1
    G = 2 * NEIGHBOURS * D
    NH = 2 * NEIGHBOURS * HEADS
    BOUND = EPS_DEN * HD
    SQUARE_SCALE = (BOUND / D) ** 0.5

    with ExitStack() as stack:
        def sb(name, shape, dt=F32):
            return stack.enter_context(nc.sbuf_tensor(name, shape, dt))

        def sem(name):
            return stack.enter_context(nc.semaphore(name))

        wq = sb("wq", [P, C, D])
        wkv = sb("wkv", [P, C, 2 * D])
        wo = sb("wo", [P, C, D])
        gq = sb("gq", [P, C])
        gkv = sb("gkv", [P, C])
        ident = sb("ident", [P, P])
        index_all = sb("index_all", [P, T], I32)
        index_part = sb("index_part", [P, T // P], I32)
        key_int = sb("key_int", [P, 1], I32)
        key = sb("key", [P, 1])
        reach_part = sb("reach_part", [P, 1])
        reach_max = sb("reach_max", [1, 1])
        beyond = sb("beyond", [1, 1], I32)
        cx = sb("cx", [P, D])
        cx_sq = sb("cx_sq", [P, D])
        cx_t = sb("cx_t", [P, C, P])
        cx_tg = sb("cx_tg", [P, C, P])
        norm = sb("norm", [P, 8])
        scaled = sb("scaled", [P, 2 * D])
        table_hi = sb("table_hi", [P, 2, D], F32R)
        table_lo = sb("table_lo", [P, 2, D], F32R)
        xs = sb("xs", [P, T // P, D])
        xt = sb("xt", [P, 2, C, PAIR])
        x_sq = sb("x_sq", [P, D])
        bound = sb("bound", [P, T // P])
        onehot = sb("onehot", [P, 2, NEIGHBOURS, PAIR], F32R)
        q = sb("q", [P, 2, 2, D])
        prod = sb("prod", [P, G])
        score = sb("score", [P, NH])
        weight = sb("weight", [P, NH])
        total = sb("total", [P, 2 * HEADS])
        total_b = sb("total_b", [P, 2 * HEADS])
        inverse = sb("inverse", [P, 2 * HEADS])
        weight_n = sb("weight_n", [P, NH])
        wv = sb("wv", [P, 2, G])
        part = sb("part", [P, 2, D])
        o = sb("o", [P, 2, 2, D])
        o_t = sb("o_t", [P, 2, C, PAIR])
        y_sb = sb("y_sb", [P, 2, 2, D])
        far_key = sb("far_key", [P, 1])
        far_hi = sb("far_hi", [P, 2, D], F32R)
        far_lo = sb("far_lo", [P, 2, D], F32R)
        far_onehot = sb("far_onehot", [P, NEIGHBOURS, PAIR], F32R)
        far_start = sb("far_start", [P, 2])
        far_k = sb("far_k", [P, PAIRS, G])
        far_v = sb("far_v", [P, PAIRS, G])

        ps_k = stack.enter_context(nc.psum_tensor("ps_k", [P, G], F32))
        ps_v = stack.enter_context(nc.psum_tensor("ps_v", [P, G], F32))
        ps_qy = stack.enter_context(nc.psum_tensor("ps_qy", [P, 2, D], F32))
        ps_t = stack.enter_context(nc.psum_tensor("ps_t", [P, C, PAIR], F32))

        in_table = sem("in_table")
        in_index = sem("in_index")
        in_index_rest = sem("in_index_rest")
        in_index_part = sem("in_index_part")
        in_q = sem("in_q")
        in_o = sem("in_o")
        in_x = [sem("in_x_even"), sem("in_x_odd")]
        stored = sem("stored")
        ident_zero = sem("ident_zero")
        ident_ready = sem("ident_ready")
        key_int_ready = sem("key_int_ready")
        key_ready = sem("key_ready")
        part_max_ready = sem("part_max_ready")
        part_max_turned = sem("part_max_turned")
        max_ready = sem("max_ready")
        beyond_ready = sem("beyond_ready")
        wq_ready = sem("wq_ready")
        cx_tg_ready = sem("cx_tg_ready")
        cx_summed = sem("cx_summed")
        norm_step = sem("norm_step")
        root_ready = sem("root_ready")
        kv_ready = sem("kv_ready")
        scaled_ready = sem("scaled_ready")
        hi_ready = sem("hi_ready")
        table_ready = sem("table_ready")
        onehot_ready = sem("onehot_ready")
        q_ready = sem("q_ready")
        q_copied = sem("q_copied")
        bound_ready = sem("bound_ready")
        k_picked = sem("k_picked")
        v_picked = sem("v_picked")
        multiplied = sem("multiplied")
        scored = sem("scored")
        weighed = sem("weighed")
        totalled = sem("totalled")
        bounded = sem("bounded")
        inverted = sem("inverted")
        normalised = sem("normalised")
        v_weighed = sem("v_weighed")
        half_summed = sem("half_summed")
        summed = sem("summed")
        turned = sem("turned")
        turned_copied = sem("turned_copied")
        y_ready = sem("y_ready")
        y_copied = sem("y_copied")
        finished = sem("finished")
        far_in = sem("far_in")
        far_cleared = sem("far_cleared")
        far_key_ready = sem("far_key_ready")
        far_cx_tg = sem("far_cx_tg")
        far_cx_summed = sem("far_cx_summed")
        far_norm_step = sem("far_norm_step")
        far_root = sem("far_root")
        far_kv = sem("far_kv")
        far_scaled = sem("far_scaled")
        far_hi_ready = sem("far_hi_ready")
        far_table_ready = sem("far_table_ready")
        far_onehot_ready = sem("far_onehot_ready")
        far_picked = sem("far_picked")
        far_added = sem("far_added")
        far_k_joined = sem("far_k_joined")
        far_v_joined = sem("far_v_joined")

        block = stack.enter_context(nc.Block())

        x_tiles = x.rearrange("(n p) d -> p n d", p=P)
        y_tiles = y.rearrange("(n p) d -> p n d", p=P)
        x_t_tiles = x_t.rearrange("(c p) t -> p c t", p=P)
        ctx_t_tiles = ctx_t.rearrange("(c p) k -> p c k", p=P)

        def reach(eng, semaphore, value):
            if not isinstance(value, int) or value > 0:
                eng.wait_ge(semaphore, value)

        @block.sync
        def _(sp):
            sp.dma_start(cx_t[:], ctx_t_tiles[:, :, 0:P]).then_inc(in_table, 16)
            sp.dma_start(gkv[:], gamma_kv).then_inc(in_table, 16)
            sp.dma_start(index_part[:], index_cols).then_inc(in_index_part, 16)
            sp.dma_start(wkv[:], wkv_t.rearrange("(c p) n -> p c n", p=P)).then_inc(in_table, 16)

            def load(p):
                if p >= 2:
                    sp.wait_ge(in_x[p % 2], 32 * (p // 2))
                    sp.wait_ge(q_ready, p - 1)
                sp.dma_start(xt[:, p % 2], x_t_tiles[:, :, p * PAIR:(p + 1) * PAIR]).then_inc(in_x[p % 2], 16)
                sp.dma_start(xs[:, 2 * p:2 * p + 2], x_tiles[:, 2 * p:2 * p + 2]).then_inc(in_x[p % 2], 16)

            def store(p):
                sp.wait_ge(finished, p + 1)
                sp.dma_start(y_tiles[:, 2 * p:2 * p + 2], xs[:, 2 * p:2 * p + 2]).then_inc(stored, 16)

            load(0)
            load(1)

            sp.wait_ge(beyond_ready, 1)
            is_beyond = sp.value_load(beyond[0:1, 0:1], min_val=0, max_val=1)
            with sp.If(is_beyond > 0):
                with sp.Fori(1, BLOCKS) as b:
                    sp.wait_ge(table_ready, 1)
                    sp.wait_ge(far_table_ready, b)
                    sp.dma_start(cx_t[:], ctx_t_tiles[:, :, bass.ds(b * P, P)]).then_inc(far_in, 16)
                    sp.dma_start(cx[:], ctx[bass.ds(b * P, P), :]).then_inc(far_in, 16)

            for p in range(PAIRS + 2):
                if p + 2 <= LAST:
                    load(p + 2)
                if p >= 2:
                    store(p - 2)
            sp.wait_ge(stored, 16 * PAIRS)

        @block.scalar
        def _(act):
            act.dma_start(index_all[:, 0:PAIR], index_row[:, 0:PAIR].broadcast_to([P, PAIR])).then_inc(in_index, 16)
            act.dma_start(cx[:], ctx[0:P, :]).then_inc(in_table, 16)
            act.dma_start(wq[:], wq_t.rearrange("(c p) n -> p c n", p=P)).then_inc(in_q, 16)
            act.dma_start(gq[:], gamma_q).then_inc(in_q, 16)
            act.dma_start(wo[:], wo_t.rearrange("(c p) n -> p c n", p=P)).then_inc(in_o, 16)
            act.dma_start(index_all[:, PAIR:T], index_row[:, PAIR:T].broadcast_to([P, T - PAIR])).then_inc(in_index_rest, 16)

            act.wait_ge(in_table, 64)
            nc.scalar.activation(cx_sq[:], cx[:], ACT.Square, accum_out=norm[:, 0:1]).then_inc(cx_summed, 1)
            act.wait_ge(norm_step, 1)
            nc.scalar.activation(norm[:, 2:3], norm[:, 1:2], ACT.Sqrt).then_inc(root_ready, 1)

            act.wait_ge(beyond_ready, 1)
            is_beyond = act.value_load(beyond[0:1, 0:1], min_val=0, max_val=1)
            with act.If(is_beyond > 0):
                with act.Fori(1, BLOCKS) as b:
                    act.wait_ge(far_in, b * 32)
                    nc.scalar.activation(cx_sq[:], cx[:], ACT.Square, accum_out=norm[:, 0:1]).then_inc(far_cx_summed, 1)
                    act.wait_ge(far_norm_step, b * 4 - 3)
                    nc.scalar.activation(norm[:, 2:3], norm[:, 1:2], ACT.Sqrt).then_inc(far_root, 1)

            def squares(p):
                act.wait_ge(in_x[p % 2], 32 * (p // 2 + 1))
                for n in (2 * p, 2 * p + 1):
                    reach(act, bound_ready, n)
                    nc.scalar.activation(x_sq[:], xs[:, n], ACT.Square, scale=SQUARE_SCALE,
                                         accum_out=bound[:, n:n + 1]).then_inc(bound_ready, 1)

            def copy_q(p):
                act.wait_ge(q_ready, p + 1)
                reach(act, multiplied, p - 1)
                nc.scalar.activation(q[:, p % 2], ps_qy[:], ACT.Copy).then_inc(q_copied, 1)

            def copy_turned(p):
                act.wait_ge(turned, p + 1)
                reach(act, y_ready, p - 1)
                nc.scalar.activation(o_t[:, p % 2], ps_t[:], ACT.Copy).then_inc(turned_copied, 1)

            def copy_y(p):
                act.wait_ge(y_ready, p + 1)
                reach(act, finished, p - 1)
                nc.scalar.activation(y_sb[:, p % 2], ps_qy[:], ACT.Copy).then_inc(y_copied, 1)

            copy_q(0)
            squares(0)
            copy_q(1)
            squares(1)
            for p in range(PAIRS + 2):
                if p >= 2:
                    copy_y(p - 2)
                if 1 <= p <= PAIRS:
                    copy_turned(p - 1)
                if p + 2 <= LAST:
                    copy_q(p + 2)
                    squares(p + 2)

        @block.vector
        def _(dve):
            def scale_context(arrived, count, done):
                dve.wait_ge(arrived, count)
                for c in range(C):
                    nc.vector.tensor_scalar(cx_tg[:, c], cx_t[:, c], gkv[:, c:c + 1], None, ALU.mult).then_inc(done, 1)

            def invert_norm(summed_rows, rooted, step, count, base):
                dve.wait_ge(summed_rows, count)
                nc.vector.tensor_scalar(norm[:, 1:2], norm[:, 0:1], 1.0 / D, EPS_RMS, ALU.mult, ALU.add).then_inc(step, 1)
                dve.wait_ge(rooted, count)
                nc.vector.reciprocal(norm[:, 3:4], norm[:, 2:3]).then_inc(step, 1)
                dve.wait_ge(step, base + 2)
                nc.vector.scalar_tensor_tensor(out=norm[:, 4:5], in0=norm[:, 3:4], scalar=norm[:, 1:2],
                                               in1=norm[:, 2:3], op0=ALU.mult, op1=ALU.add).then_inc(step, 1)
                dve.wait_ge(step, base + 3)
                nc.vector.reciprocal(norm[:, 5:6], norm[:, 4:5]).then_inc(step, 1)
                dve.wait_ge(step, base + 4)

            def build_table(projected, scaled, hi, lo, scaled_done, hi_done, done, count):
                dve.wait_ge(projected, count)
                nc.vector.tensor_scalar(scaled, ps_v[:, 0:2 * D], norm[:, 5:6], 2.0, ALU.mult,
                                        ALU.mult).then_inc(scaled_done, 1)
                dve.wait_ge(scaled_done, count)
                nc.vector.tensor_copy(hi, scaled.rearrange("p (a d) -> p a d", a=2)).then_inc(hi_done, 1)
                dve.wait_ge(hi_done, count)
                nc.vector.tensor_tensor(lo, scaled.rearrange("p (a d) -> p a d", a=2), hi.bitcast(F32), ALU.subtract).then_inc(done, 1)

            dve.wait_ge(in_index_part, 16)
            nc.vector.tensor_reduce(reach_part[:], index_part[:], AX_X, ALU.max).then_inc(part_max_ready, 1)

            scale_context(in_table, 64, cx_tg_ready)
            dve.wait_ge(in_q, 32)
            for c in range(C):
                nc.vector.tensor_scalar(wq[:, c], wq[:, c], gq[:, c:c + 1], None, ALU.mult).then_inc(wq_ready, 1)
            dve.wait_ge(key_int_ready, 1)
            nc.vector.tensor_copy(key[:], key_int[:]).then_inc(key_ready, 1)
            dve.wait_ge(part_max_turned, 1)
            nc.vector.tensor_reduce(reach_max[:], ps_t[0:1, 0, 0:P], AX_X, ALU.max).then_inc(max_ready, 1)
            dve.wait_ge(max_ready, 1)
            nc.vector.tensor_scalar(beyond[:], reach_max[:], float(P - 2), None, ALU.is_gt).then_inc(beyond_ready, 1)
            invert_norm(cx_summed, root_ready, norm_step, 1, 0)

            build_table(kv_ready, scaled[:], table_hi[:], table_lo[:], scaled_ready, hi_ready, table_ready, 1)

            dve.wait_ge(beyond_ready, 1)
            is_beyond = dve.value_load(beyond[0:1, 0:1], min_val=0, max_val=1)
            with dve.If(is_beyond > 0):
                dve.wait_ge(in_index_rest, 16)
                dve.wait_ge(in_index, 16)
                nc.vector.memset(far_k[:], 0.0).then_inc(far_cleared, 1)
                nc.vector.memset(far_v[:], 0.0).then_inc(far_cleared, 1)
                nc.vector.tensor_copy(far_key[:], key[:]).then_inc(far_key_ready, 1)
                dve.wait_ge(far_cleared, 2)
                dve.wait_ge(far_key_ready, 1)
                nc.vector.memset(far_start[:, 0:1], 0.0).then_inc(far_added, 2)
                nc.vector.memset(far_start[:, 1:2], 0.0).then_inc(far_table_ready, 1)
                with dve.Fori(1, BLOCKS) as b:
                    scale_context(far_in, b * 32, far_cx_tg)
                    nc.vector.tensor_scalar(far_key[:], far_key[:], float(P), None, ALU.add).then_inc(far_key_ready, 1)
                    dve.wait_ge(far_key_ready, b + 1)
                    invert_norm(far_cx_summed, far_root, far_norm_step, b, b * 4 - 4)
                    build_table(far_kv, scaled[:], far_hi[:], far_lo[:], far_scaled, far_hi_ready, far_table_ready, b)
                    with dve.Fori(0, PAIRS) as p:
                        for j in range(NEIGHBOURS):
                            nc.vector.tensor_scalar(far_onehot[:, j], index_all[:, bass.ds(p * PAIR, PAIR)],
                                                    far_key[:, 0:1], float(1 - j), ALU.subtract,
                                                    ALU.is_equal).then_inc(far_onehot_ready, 1)
                        dve.wait_ge(far_picked, (b - 1) * PAIRS + p + 1)
                        nc.vector.tensor_tensor(far_k[:, bass.ds(p, 1)].rearrange("p a g -> p (a g)"),
                                                far_k[:, bass.ds(p, 1)].rearrange("p a g -> p (a g)"), ps_k[:],
                                                ALU.add).then_inc(far_added, 1)
                        nc.vector.tensor_tensor(far_v[:, bass.ds(p, 1)].rearrange("p a g -> p (a g)"),
                                                far_v[:, bass.ds(p, 1)].rearrange("p a g -> p (a g)"), ps_v[:],
                                                ALU.add).then_inc(far_added, 1)
                dve.wait_ge(far_added, 2 + 2 * PAIRS * (BLOCKS - 1))

            by_pair = "p (a j d) -> p a j d"

            def add_far(ps, far, p, before, count, done):
                with dve.If(is_beyond > 0):
                    dve.wait_ge(before, count)
                    nc.vector.tensor_tensor(ps[:], ps[:], far[:, p], ALU.add).then_inc(done, 1)
                    dve.wait_ge(done, p + 1)

            def attend(p):
                dve.wait_ge(k_picked, p + 1)
                dve.wait_ge(q_copied, p + 1)
                reach(dve, scored, p)
                add_far(ps_k, far_k, p, k_picked, p + 1, far_k_joined)
                nc.vector.tensor_tensor(prod[:].rearrange(by_pair, a=2, j=NEIGHBOURS),
                                        ps_k[:].rearrange(by_pair, a=2, j=NEIGHBOURS),
                                        q[:, p % 2].unsqueeze(2).to_broadcast([P, 2, NEIGHBOURS, D]),
                                        ALU.mult).then_inc(multiplied, 1)
                dve.wait_ge(multiplied, p + 1)
                reach(dve, weighed, p)
                nc.vector.tensor_reduce(score[:], prod[:].rearrange("p (n d) -> p n d", d=HD), AX_X,
                                        ALU.add).then_inc(scored, 1)
                dve.wait_ge(scored, p + 1)
                nc.vector.scalar_tensor_tensor(out=weight[:], in0=score[:], scalar=0.0, in1=score[:], op0=ALU.max,
                                               op1=ALU.mult).then_inc(weighed, 1)
                dve.wait_ge(weighed, p + 1)
                nc.vector.tensor_reduce(total[:].rearrange("p (a h) -> p a h", a=2),
                                        weight[:].rearrange("p (a j h) -> p a h j", a=2, j=NEIGHBOURS), AX_X,
                                        ALU.add).then_inc(totalled, 1)
                dve.wait_ge(totalled, p + 1)
                dve.wait_ge(bound_ready, 2 * p + 2)
                nc.vector.scalar_tensor_tensor(out=total_b[:].rearrange("p (a h) -> p a h", a=2),
                                               in0=bound[:, 2 * p:2 * p + 2].unsqueeze(2).to_broadcast([P, 2, HEADS]),
                                               scalar=BOUND * EPS_RMS,
                                               in1=total[:].rearrange("p (a h) -> p a h", a=2), op0=ALU.add,
                                               op1=ALU.max).then_inc(bounded, 1)
                dve.wait_ge(bounded, p + 1)
                nc.vector.reciprocal(inverse[:], total_b[:]).then_inc(inverted, 1)
                dve.wait_ge(inverted, p + 1)
                nc.vector.tensor_tensor(weight_n[:].rearrange("p (a j h) -> p a j h", a=2, j=NEIGHBOURS),
                                        weight[:].rearrange("p (a j h) -> p a j h", a=2, j=NEIGHBOURS),
                                        inverse[:].rearrange("p (a h) -> p a h", a=2).unsqueeze(2).to_broadcast([P, 2, NEIGHBOURS, HEADS]),
                                        ALU.mult).then_inc(normalised, 1)
                dve.wait_ge(normalised, p + 1)
                dve.wait_ge(v_picked, p + 1)
                reach(dve, summed, p - 1)
                add_far(ps_v, far_v, p, v_picked, p + 1, far_v_joined)
                nc.vector.tensor_tensor(wv[:, p % 2].rearrange("p (n d) -> p n d", d=HD),
                                        ps_v[:].rearrange("p (n d) -> p n d", d=HD),
                                        weight_n[:].unsqueeze(2).to_broadcast([P, NH, HD]),
                                        ALU.mult).then_inc(v_weighed, 1)

            for p in range(PAIRS):
                attend(p)

        @block.gpsimd
        def _(pool):
            nc.gpsimd.iota(key_int[:], [[0, 1]], base=0, channel_multiplier=1).then_inc(key_int_ready, 1)
            nc.gpsimd.memset(ident[:], 0.0).then_inc(ident_zero, 1)
            pool.wait_ge(ident_zero, 1)
            nc.gpsimd.affine_select(out=ident[:], in_=ident[:], compare_op=ALU.not_equal, fill=1.0, base=0,
                                    pattern=[[-1, P]], channel_multiplier=1).then_inc(ident_ready, 1)
            pool.wait_ge(key_ready, 1)

            def find(p):
                pool.wait_ge(in_index if p == 0 else in_index_rest, 16)
                reach(pool, v_picked, p - 1)
                for j in range(NEIGHBOURS):
                    nc.gpsimd.tensor_scalar(onehot[:, p % 2, j], index_all[:, p * PAIR:(p + 1) * PAIR], key[:, 0:1],
                                            float(1 - j), ALU.subtract, ALU.is_equal).then_inc(onehot_ready, 1)

            def sum_neighbours(p):
                pool.wait_ge(v_weighed, p + 1)
                reach(pool, summed, p)
                w = wv[:, p % 2].rearrange(by_pair_pool, a=2, j=NEIGHBOURS)
                nc.gpsimd.tensor_tensor(part[:], w[:, :, 0], w[:, :, 1], ALU.add).then_inc(half_summed, 1)
                pool.wait_ge(half_summed, p + 1)
                reach(pool, turned, p - 1)
                nc.gpsimd.tensor_tensor(o[:, p % 2], part[:], w[:, :, 2], ALU.add).then_inc(summed, 1)

            def add_x(p):
                pool.wait_ge(y_copied, p + 1)
                nc.gpsimd.tensor_tensor(xs[:, 2 * p:2 * p + 2], xs[:, 2 * p:2 * p + 2], y_sb[:, p % 2],
                                        ALU.add).then_inc(finished, 1)

            by_pair_pool = "p (a j d) -> p a j d"
            find(0)
            find(1)
            for p in range(PAIRS + 2):
                if 1 <= p <= PAIRS:
                    sum_neighbours(p - 1)
                if p + 2 <= LAST:
                    find(p + 2)
                if p >= 2:
                    add_x(p - 2)

        @block.tensor
        def _(pe):
            def project_context(ready, count, done):
                pe.wait_ge(ready, count)
                for c in range(C):
                    last = nc.tensor.matmul(ps_v[:, 0:2 * D], cx_tg[:, c], wkv[:, c], start=c == 0, stop=c == C - 1)
                last.then_inc(done, 1)

            def pick(ps, onehots, hi, lo, which):
                for a in range(2):
                    for j in range(NEIGHBOURS):
                        at = (a * NEIGHBOURS + j) * D
                        rows = onehots[:, j, a * P:(a + 1) * P]
                        nc.tensor.matmul(ps[:, at:at + D], rows, hi[:, which], start=True, stop=False)
                        last = nc.tensor.matmul(ps[:, at:at + D], rows, lo[:, which], start=False, stop=True)
                return last

            def project_q(p):
                pe.wait_ge(in_x[p % 2], 32 * (p // 2 + 1))
                if p == 0:
                    pe.wait_ge(wq_ready, C)
                reach(pe, q_copied, p)
                reach(pe, y_copied, p - 3)
                for a in range(2):
                    for c in range(C):
                        last = nc.tensor.matmul(ps_qy[:, a], xt[:, p % 2, c, a * P:(a + 1) * P], wq[:, c],
                                                start=c == 0, stop=c == C - 1)
                last.then_inc(q_ready, 1)

            def pick_keys(p):
                pe.wait_ge(onehot_ready, NEIGHBOURS * (p + 1))
                reach(pe, multiplied, p)
                pick(ps_k, onehot[:, p % 2], table_hi, table_lo, 0).then_inc(k_picked, 1)

            def pick_values(p):
                reach(pe, v_weighed, p)
                pick(ps_v, onehot[:, p % 2], table_hi, table_lo, 1).then_inc(v_picked, 1)

            def turn(p):
                pe.wait_ge(summed, p + 1)
                reach(pe, turned_copied, p)
                for a in range(2):
                    for c in range(C):
                        last = nc.tensor.transpose(ps_t[:, c, a * P:(a + 1) * P], o[:, p % 2, a, c * P:(c + 1) * P], ident[:])
                last.then_inc(turned, 1)

            def project_out(p):
                pe.wait_ge(turned_copied, p + 1)
                pe.wait_ge(q_copied, min(p + 4, PAIRS))
                reach(pe, y_copied, p)
                if p == 0:
                    pe.wait_ge(in_o, 16)
                for a in range(2):
                    for c in range(C):
                        last = nc.tensor.matmul(ps_qy[:, a], o_t[:, p % 2, c, a * P:(a + 1) * P], wo[:, c],
                                                start=c == 0, stop=c == C - 1)
                last.then_inc(y_ready, 1)

            pe.wait_ge(part_max_ready, 1)
            pe.wait_ge(ident_ready, 1)
            nc.tensor.transpose(ps_t[0:1, 0, 0:P], reach_part[:], ident[:]).then_inc(part_max_turned, 1)
            project_context(cx_tg_ready, C, kv_ready)

            project_q(0)
            pe.wait_ge(beyond_ready, 1)
            is_beyond = pe.value_load(beyond[0:1, 0:1], min_val=0, max_val=1)
            with pe.If(is_beyond > 0):
                with pe.Fori(1, BLOCKS) as b:
                    pe.wait_ge(far_added, (b - 1) * (2 * PAIRS) + 2)
                    pe.wait_ge(table_ready, 1)
                    project_context(far_cx_tg, b * C, far_kv)
                    with pe.Fori(0, PAIRS) as p:
                        pe.wait_ge(far_table_ready, b + 1)
                        pe.wait_ge(far_onehot_ready, ((b - 1) * PAIRS + p) * NEIGHBOURS + NEIGHBOURS)
                        pe.wait_ge(far_added, ((b - 1) * PAIRS + p) * 2 + 2)
                        pick(ps_k, far_onehot, far_hi, far_lo, 0)
                        pick(ps_v, far_onehot, far_hi, far_lo, 1).then_inc(far_picked, 1)
                pe.wait_ge(far_added, 2 + 2 * PAIRS * (BLOCKS - 1))

            pe.wait_ge(table_ready, 1)
            pick_keys(0)
            pick_values(0)
            project_q(1)
            for p in range(PAIRS + 2):
                if p >= 2:
                    project_out(p - 2)
                if p + 1 <= LAST:
                    pick_keys(p + 1)
                if 1 <= p <= PAIRS:
                    turn(p - 1)
                if p + 2 <= LAST:
                    project_q(p + 2)
                if p + 1 <= LAST:
                    pick_values(p + 1)


def kernel(x, ctx_1024, itok_BxS_0_255, L0_xattn_gamma_q, L0_xattn_gamma_kv, L0_xattn_Wq, L0_xattn_Wk, L0_xattn_Wv,
           L0_xattn_Wo):
    import concourse.bacc as bacc
    from concourse.bass_utils import run_bass_kernel_spmd

    x = np.asarray(x)
    ctx = np.asarray(ctx_1024)[0]
    ctx = np.pad(ctx, ((0, -len(ctx) % P), (0, 0)))
    index = np.asarray(itok_BxS_0_255)
    arrays = {
        "x": x[0],
        "x_t": x[0].T,
        "ctx": ctx,
        "ctx_t": ctx.T,
        "index_row": index,
        "index_cols": index.reshape(P, -1),
        "gamma_q": np.asarray(L0_xattn_gamma_q).reshape(-1, P).T,
        "gamma_kv": np.asarray(L0_xattn_gamma_kv).reshape(-1, P).T,
        "wq_t": np.asarray(L0_xattn_Wq).T,
        "wkv_t": np.concatenate([np.asarray(L0_xattn_Wk).T, np.asarray(L0_xattn_Wv).T], axis=1),
        "wo_t": np.asarray(L0_xattn_Wo).T,
    }
    arrays = {name: np.ascontiguousarray(a) for name, a in arrays.items()}
    nc = bacc.Bacc("TRN2", target_bir_lowering=False, num_devices=1)
    args = {n: nc.dram_tensor(n, a.shape, mybir.dt.from_np(a.dtype), kind="ExternalInput").ap()
            for n, a in arrays.items()}
    y = nc.dram_tensor("y", x[0].shape, F32, kind="ExternalOutput").ap()
    local_attention(nc, y=y, **args)
    r = run_bass_kernel_spmd(nc, [arrays], core_ids=[0])
    return r.results[0]["y"].reshape(x.shape)
```

```python
from contextlib import ExitStack

import numpy as np

import concourse.bass as bass
from concourse import mybir

F32 = mybir.dt.float32
F32R = mybir.dt.float32r
I32 = mybir.dt.int32
ALU = mybir.AluOpType
ACT = mybir.ActivationFunctionType
AX_X = mybir.AxisListType.X

P = 128
EPS_RMS = 1.1920929e-07
EPS_DEN = 1e-06
HEADS = 16
NEIGHBOURS = 3
KEYS = 1601
HALF = P // 2
BLOCKS = -(-(KEYS + 1) // HALF)
ALIAS = BLOCKS * HALF - 1
ROWS = BLOCKS * HALF + 2


def local_attention(nc, x, x_t, ctx, ctx_t, index_row, index_cols, wq_t, wkv_t, wo_t, y):
    T, D = x.shape
    HD = D // HEADS
    C = D // P
    PAIR = 2 * P
    PAIRS = T // PAIR
    LAST = PAIRS - 1
    ND = NEIGHBOURS * D
    G = 2 * ND
    NH = 2 * NEIGHBOURS * HEADS
    BOUND = EPS_DEN * HD
    SQUARE_SCALE = (BOUND / D) ** 0.5

    with ExitStack() as stack:
        def sb(name, shape, dt=F32):
            return stack.enter_context(nc.sbuf_tensor(name, shape, dt))

        def sem(name):
            return stack.enter_context(nc.semaphore(name))

        wq = sb("wq", [P, C, D])
        wkv = sb("wkv", [P, C, 2 * D])
        wo = sb("wo", [P, C, D])
        ident = sb("ident", [P, P])
        zeros = sb("zeros", [P, P])
        zeros_root = sb("zeros_root", [P, 1])
        index_all = sb("index_all", [P, T], I32)
        index_part = sb("index_part", [P, T // P], I32)
        key_int = sb("key_int", [P, 1], I32)
        key_half = sb("key_half", [P, 1])
        key = sb("key", [P, 1])
        off_centre = sb("off_centre", [P, T // P])
        reach_part = sb("reach_part", [P, 1])
        reach_max = sb("reach_max", [1, 1])
        beyond = sb("beyond", [1, 1], I32)
        cx = sb("cx", [P, NEIGHBOURS, D])
        cx_sq = sb("cx_sq", [P, D])
        gammas_cx_t = sb("gammas_cx_t", [P, C, 2 + HALF + 2])
        gq, gkv, cx_t = gammas_cx_t[:, :, 0:1], gammas_cx_t[:, :, 1:2], gammas_cx_t[:, :, 2:]
        cx_tg = sb("cx_tg", [P, C, NEIGHBOURS, 2, HALF])
        table = sb("table", [P, 2, ND], F32R)
        sums = sb("sums", [P, NEIGHBOURS])
        mean_4th = sb("mean_4th", [P, NEIGHBOURS])
        half_root = sb("half_root", [P, NEIGHBOURS])
        half_root_inv = sb("half_root_inv", [P, NEIGHBOURS])
        ratio = sb("ratio", [P, NEIGHBOURS])
        root = sb("root", [P, NEIGHBOURS])
        rescale = sb("rescale", [P, NEIGHBOURS])
        xs = sb("xs", [P, T // P, D])
        xt = sb("xt", [P, 2, C, PAIR])
        x_sq = sb("x_sq", [P, D])
        bound = sb("bound", [P, T // P])
        onehot = sb("onehot", [P, T], F32R)
        q = sb("q", [P, 2, 2, D])
        prod = sb("prod", [P, G])
        score = sb("score", [P, 2, NH])
        positive = sb("positive", [P, NH])
        weight = sb("weight", [P, 2, NH])
        total = sb("total", [P, 2 * HEADS])
        total_b = sb("total_b", [P, 2 * HEADS])
        inverse = sb("inverse", [P, 2 * HEADS])
        weight_n = sb("weight_n", [P, 2, NH])
        wv = sb("wv", [P, 2, G])
        part = sb("part", [P, 2, D])
        last_part = sb("last_part", [P, 2, D])
        o = sb("o", [P, 2, 2, D])
        o_t = sb("o_t", [P, 2, C, PAIR])
        y_sb = sb("y_sb", [P, 2, 2, D])
        scaled_v = wv[:, 1, 0:ND]
        far_cx_t = sb("far_cx_t", [P, C, HALF + 2])
        far_cx = wv[:, 0, 0:ND].rearrange("p (j d) -> p j d", j=NEIGHBOURS)
        far_cx_tg = prod[:, 0:C * NEIGHBOURS * P].rearrange("p (c j a v) -> p c j a v", c=C, j=NEIGHBOURS, a=2)
        far_table = sb("far_table", [P, 2, ND], F32R)
        far_rescale = sb("far_rescale", [P, NEIGHBOURS])
        far_key = sb("far_key", [P, 1])
        far_onehot = sb("far_onehot", [P, PAIR], F32R)
        far_alias = sb("far_alias", [P, PAIR])
        far_index = sb("far_index", [P, PAIR])
        far_start = sb("far_start", [P, 1])
        far_k = sb("far_k", [P, PAIRS, G])
        far_v = sb("far_v", [P, PAIRS, G])

        ps_k = stack.enter_context(nc.psum_tensor("ps_k", [P, G], F32))
        ps_v = stack.enter_context(nc.psum_tensor("ps_v", [P, G], F32))
        ps_qy = stack.enter_context(nc.psum_tensor("ps_qy", [P, 2, D], F32))
        ps_t = stack.enter_context(nc.psum_tensor("ps_t", [P, C, PAIR], F32))

        in_index_part = sem("in_index_part")
        in_cx = sem("in_cx")
        in_cx_t = sem("in_cx_t")
        in_index = sem("in_index")
        in_index_rest = sem("in_index_rest")
        in_k = sem("in_k")
        in_v = sem("in_v")
        in_q = sem("in_q")
        in_o = sem("in_o")
        in_x_t = [sem("in_x_t_even"), sem("in_x_t_odd")]
        in_x = [sem("in_x_even"), sem("in_x_odd")]
        stored = sem("stored")
        zeros_ready = sem("zeros_ready")
        ident_zero = sem("ident_zero")
        ident_ready = sem("ident_ready")
        key_int_ready = sem("key_int_ready")
        key_half_ready = sem("key_half_ready")
        key_ready = sem("key_ready")
        off_centre_ready = sem("off_centre_ready")
        reach_part_ready = sem("reach_part_ready")
        reach_part_turned = sem("reach_part_turned")
        max_ready = sem("max_ready")
        beyond_ready = sem("beyond_ready")
        wq_ready = sem("wq_ready")
        cx_tg_ready = sem("cx_tg_ready")
        rows_squared = sem("rows_squared")
        mean_ready = sem("mean_ready")
        half_root_ready = sem("half_root_ready")
        half_root_inv_ready = sem("half_root_inv_ready")
        ratio_ready = sem("ratio_ready")
        root_ready = sem("root_ready")
        rescale_ready = sem("rescale_ready")
        k_table = dict(projected=sem("k_projected"), rounded=sem("k_rounded"), ready=sem("k_table_ready"))
        scaled_v_ready = sem("scaled_v_ready")
        v_table = dict(projected=sem("v_projected"), rounded=sem("v_rounded"), ready=sem("v_table_ready"))
        far_v_table = dict(projected=sem("far_v_projected"), rounded=sem("far_v_rounded"),
                           ready=sem("far_v_table_ready"))
        onehot_ready = sem("onehot_ready")
        q_ready = sem("q_ready")
        q_copied = sem("q_copied")
        bound_ready = sem("bound_ready")
        k_picked = sem("k_picked")
        v_picked = sem("v_picked")
        multiplied = sem("multiplied")
        scored = sem("scored")
        clipped = sem("clipped")
        weighed = sem("weighed")
        totalled = sem("totalled")
        bounded = sem("bounded")
        inverted = sem("inverted")
        normalised = sem("normalised")
        v_weighed = sem("v_weighed")
        half_summed = sem("half_summed")
        summed = sem("summed")
        turned = sem("turned")
        turned_copied = sem("turned_copied")
        y_ready = sem("y_ready")
        y_copied = sem("y_copied")
        finished = sem("finished")
        first_v_weighed = sem("first_v_weighed")
        last_v_weighed = sem("last_v_weighed")
        last_half_summed = sem("last_half_summed")
        last_summed = sem("last_summed")
        last_turned = sem("last_turned")
        last_turned_copied = sem("last_turned_copied")
        last_y_ready = sem("last_y_ready")
        last_finished = sem("last_finished")
        far_in = sem("far_in")
        far_cleared = sem("far_cleared")
        far_key_ready = sem("far_key_ready")
        far_alias_ready = sem("far_alias_ready")
        far_index_ready = sem("far_index_ready")
        far_onehot_ready = sem("far_onehot_ready")
        far_picked = sem("far_picked")
        far_added = sem("far_added")
        far_k_joined = sem("far_k_joined")
        far_v_joined = sem("far_v_joined")

        block = stack.enter_context(nc.Block())

        x_tiles = x.rearrange("(n p) d -> p n d", p=P)
        y_tiles = y.rearrange("(n p) d -> p n d", p=P)
        x_t_tiles = x_t.rearrange("(c p) t -> p c t", p=P)
        ctx_t_tiles = ctx_t.rearrange("(c p) k -> p c k", p=P)
        wkv_t_tiles = wkv_t.rearrange("(c p) n -> p c n", p=P)

        def rows_around(first):
            rows = ctx[bass.ds(first, HALF)]
            return bass.AP(tensor=rows.tensor, offset=rows.offset, ap=[[0, 2], [D, HALF], [1, ND]])

        FAR_LOADS = 2 * 16
        WARM_UPS = 9

        def wait_for(eng, semaphore, value):
            if not isinstance(value, int) or value > 0:
                eng.wait_ge(semaphore, value)

        BANK = 512
        last_t = [ps_v[:, a * BANK:a * BANK + D].rearrange("p (c t) -> p c t", c=C) for a in range(2)]
        last_y = [ps_v[:, 2 * BANK:2 * BANK + D], ps_k[:, 0:D]]

        by_pair = "p (a j d) -> p a j d"

        def around_indices(columns, c):
            first = columns[:, c, 0:HALF]
            return bass.AP(tensor=first.tensor, offset=first.offset,
                           ap=[first.ap[0], [1, NEIGHBOURS], [0, 2], [1, HALF]])

        def y_buffer(p):
            return q[:, (LAST - 1) % 2] if p == LAST - 2 else y_sb[:, p % 2]

        def values_bank(p):
            return ps_k if p == LAST else ps_v

        @block.sync
        def _(sp):
            sp.dma_start(cx[:], rows_around(0)).then_inc(in_cx, 16)
            sp.dma_start(wkv[:, :, 0:D], wkv_t_tiles[:, :, 0:D]).then_inc(in_k, 16)
            sp.dma_start(wq[:], wq_t.rearrange("(c p) n -> p c n", p=P)).then_inc(in_q, 16)

            def load_x_t(p):
                sp.dma_start(xt[:, p % 2], x_t_tiles[:, :, p * PAIR:(p + 1) * PAIR]).then_inc(in_x_t[p % 2], 16)

            def load_x(p):
                sp.dma_start(xs[:, 2 * p:2 * p + 2], x_tiles[:, 2 * p:2 * p + 2]).then_inc(in_x[p % 2], 16)

            def store(p):
                sp.wait_ge(finished, p + 1)
                sp.dma_start(y_tiles[:, 2 * p:2 * p + 2], xs[:, 2 * p:2 * p + 2]).then_inc(stored, 16)

            load_x_t(0)
            sp.dma_start(index_all[:, 0:PAIR], index_row[:, 0:PAIR].broadcast_to([P, PAIR])).then_inc(in_index, 16)
            load_x_t(1)
            sp.dma_start(index_all[:, PAIR:T], index_row[:, PAIR:T].broadcast_to([P, T - PAIR])).then_inc(in_index_rest, 16)
            load_x(0)
            sp.dma_start(wkv[:, :, D:2 * D], wkv_t_tiles[:, :, D:2 * D]).then_inc(in_v, 16)
            load_x(1)
            sp.dma_start(wo[:], wo_t.rearrange("(c p) n -> p c n", p=P)).then_inc(in_o, 16)

            sp.wait_ge(beyond_ready, 1)
            is_beyond = sp.value_load(beyond[0:1, 0:1], min_val=0, max_val=1)
            with sp.If(is_beyond > 0):
                with sp.Fori(1, BLOCKS) as b:
                    sp.wait_ge(cx_tg_ready, b * C)
                    sp.dma_start(far_cx_t[:], ctx_t_tiles[:, :, bass.ds(b * HALF + 2, HALF + 2)]).then_inc(far_in, 16)
                    sp.wait_ge(rows_squared, b * NEIGHBOURS)
                    sp.dma_start(far_cx, rows_around(b * HALF)).then_inc(far_in, 16)

            for p in range(2, PAIRS):
                sp.wait_ge(in_x_t[p % 2], 16 * (p // 2))
                sp.wait_ge(in_x[p % 2], 16 * (p // 2))
                sp.wait_ge(q_ready, p - 1)
                load_x_t(p)
                load_x(p)
            for p in range(LAST - 1):
                store(p)
            sp.wait_ge(last_finished, 1)
            sp.dma_start(y_tiles[:, 2 * LAST - 2:2 * LAST], xs[:, 2 * LAST - 2:2 * LAST]).then_inc(stored, 16)
            for a in range(2):
                sp.wait_ge(last_finished, a + 2)
                n = 2 * LAST + a
                sp.dma_start(y_tiles[:, n], xs[:, n]).then_inc(stored, 16)
            sp.wait_ge(stored, 16 * (PAIRS + 1))

        @block.scalar
        def _(act):
            act.dma_start(gammas_cx_t[:], ctx_t_tiles[:, :, 0:2 + HALF + 2]).then_inc(in_cx_t, 16)
            act.dma_start(index_part[:], index_cols).then_inc(in_index_part, 16)

            def scale_context(to, columns):
                for c in range(1, C, 2):
                    nc.scalar.activation(to[:, c], around_indices(columns, c), ACT.Copy,
                                         scale=gkv[:, c]).then_inc(cx_tg_ready, 1)

            def row_roots(rows, n):
                for j in range(NEIGHBOURS):
                    wait_for(act, rows_squared, n * NEIGHBOURS + j)
                    nc.scalar.activation(cx_sq[:], rows[:, j], ACT.Square,
                                         accum_out=sums[:, j:j + 1]).then_inc(rows_squared, 1)
                act.wait_ge(mean_ready, n + 1)
                nc.scalar.activation(half_root[:], mean_4th[:], ACT.Sqrt).then_inc(half_root_ready, 1)

            def round_table(to, kv, scale, steps, n):
                ps = (ps_k, ps_v)[kv]
                for j in range(NEIGHBOURS):
                    act.wait_ge(steps["projected"], n * 2 + j // 2 + 1)
                    nc.scalar.activation(to[:, kv, j * D:(j + 1) * D], ps[:, j * D:(j + 1) * D], ACT.Copy,
                                         scale=scale[:, j:j + 1]).then_inc(steps["rounded"], 1)

            act.wait_ge(zeros_ready, 1)
            nc.scalar.activation(zeros_root[:], zeros[:, 0:1], ACT.Sqrt)
            act.wait_ge(in_cx_t, 16)
            scale_context(cx_tg, cx_t)
            act.wait_ge(in_cx, 16)
            row_roots(cx, 0)
            act.wait_ge(in_q, 16)
            for c in range(C):
                nc.scalar.activation(wq[:, c], wq[:, c], ACT.Copy, scale=gq[:, c]).then_inc(wq_ready, 1)
            act.wait_ge(rescale_ready, 1)
            round_table(table, 0, rescale, k_table, 0)

            act.wait_ge(beyond_ready, 1)
            is_beyond = act.value_load(beyond[0:1, 0:1], min_val=0, max_val=1)
            with act.If(is_beyond > 0):
                with act.Fori(1, BLOCKS) as b:
                    act.wait_ge(far_in, b * FAR_LOADS)
                    scale_context(far_cx_tg, far_cx_t)
                    row_roots(far_cx, b)
                    act.wait_ge(rescale_ready, b + 1)
                    round_table(far_table, 0, far_rescale, k_table, b)
                    round_table(far_table, 1, far_rescale, far_v_table, b - 1)

            def squares(p):
                act.wait_ge(in_x[p % 2], 16 * (p // 2 + 1))
                for n in (2 * p, 2 * p + 1):
                    wait_for(act, bound_ready, n)
                    nc.scalar.activation(x_sq[:], xs[:, n], ACT.Square, scale=SQUARE_SCALE,
                                         accum_out=bound[:, n:n + 1]).then_inc(bound_ready, 1)

            def copy_q(p):
                act.wait_ge(q_ready, p + 1)
                wait_for(act, multiplied, p - 1)
                nc.scalar.activation(q[:, p % 2], ps_qy[:], ACT.Copy).then_inc(q_copied, 1)

            def copy_turned(p):
                act.wait_ge(turned, p + 1)
                wait_for(act, y_ready, p - 1)
                nc.scalar.activation(o_t[:, p % 2], ps_t[:], ACT.Copy).then_inc(turned_copied, 1)

            def copy_y(p):
                act.wait_ge(y_ready, p + 1)
                if p == LAST - 2:
                    act.wait_ge(multiplied, LAST)
                else:
                    wait_for(act, finished, p - 1)
                nc.scalar.activation(y_buffer(p), ps_qy[:], ACT.Copy).then_inc(y_copied, 1)

            def weigh(p):
                act.wait_ge(scored, p + 1)
                wait_for(act, weighed, p)
                nc.scalar.activation(positive[:], score[:, p % 2], ACT.Relu).then_inc(clipped, 1)
                act.wait_ge(clipped, p + 1)
                wait_for(act, normalised, p - 1)
                nc.scalar.activation(weight[:, p % 2], positive[:], ACT.Square).then_inc(weighed, 1)

            copy_q(0)
            squares(0)
            copy_q(1)
            squares(1)
            for p in range(LAST - 1):
                if p >= 4:
                    copy_y(p - 4)
                if p >= 3:
                    copy_turned(p - 3)
                weigh(p)
                if p == 0:
                    round_table(table, 1, rescale, v_table, 0)
                    for j in range(NEIGHBOURS):
                        at = slice(j * D, (j + 1) * D)
                        nc.scalar.activation(scaled_v[HALF:P, at], ps_v[HALF:P, at], ACT.Copy,
                                             scale=rescale[HALF:P, j:j + 1]).then_inc(scaled_v_ready, 1)
                copy_q(p + 2)
                squares(p + 2)
            copy_y(LAST - 5)
            copy_turned(LAST - 4)
            weigh(LAST - 1)
            copy_y(LAST - 4)
            copy_turned(LAST - 3)
            weigh(LAST)
            for p in (LAST - 3, LAST - 2):
                copy_y(p)
                copy_turned(p + 1)
            for a in range(2):
                act.wait_ge(last_turned, a + 1)
                nc.scalar.activation(o_t[:, LAST % 2, :, a * P:(a + 1) * P], last_t[a], ACT.Copy).then_inc(last_turned_copied, 1)

        @block.vector
        def _(dve):
            def scale_context(to, columns):
                for c in range(0, C, 2):
                    nc.vector.tensor_scalar(to[:, c], around_indices(columns, c), gkv[:, c], None,
                                            ALU.mult).then_inc(cx_tg_ready, 1)

            def take_mean(n):
                dve.wait_ge(rows_squared, (n + 1) * NEIGHBOURS)
                nc.vector.tensor_scalar(mean_4th[:], sums[:], 0.25 / D, 0.25 * EPS_RMS, ALU.mult, ALU.add).then_inc(mean_ready, 1)

            def invert_norm(to, n):
                dve.wait_ge(half_root_ready, n + 1)
                nc.vector.reciprocal(half_root_inv[:], half_root[:]).then_inc(half_root_inv_ready, 1)
                dve.wait_ge(half_root_inv_ready, n + 1)
                nc.vector.tensor_tensor(ratio[:], mean_4th[:], half_root_inv[:], ALU.mult).then_inc(ratio_ready, 1)
                dve.wait_ge(ratio_ready, n + 1)
                nc.vector.tensor_tensor(root[:], half_root[:], ratio[:], ALU.add).then_inc(root_ready, 1)
                dve.wait_ge(root_ready, n + 1)
                nc.vector.reciprocal(to[:], root[:]).then_inc(rescale_ready, 1)

            def fill_table(to, kv, scale, steps, n):
                ps = (ps_k, ps_v)[kv]
                for j in range(NEIGHBOURS):
                    at = slice(j * D, (j + 1) * D)
                    dve.wait_ge(steps["rounded"], n * NEIGHBOURS + min(j // 2 * 2 + 2, NEIGHBOURS))
                    nc.vector.scalar_tensor_tensor(out=to[HALF:P, kv, at], in0=ps[HALF:P, at],
                                                   scalar=scale[HALF:P, j:j + 1], in1=to[HALF:P, kv, at].bitcast(F32),
                                                   op0=ALU.mult, op1=ALU.subtract).then_inc(steps["ready"], 1)

            def find(first, end):
                nc.vector.tensor_scalar(onehot[:, first:end], index_all[:, first:end], key[:, 0:1], None,
                                        ALU.is_equal).then_inc(onehot_ready, 1)

            dve.wait_ge(in_cx_t, 16)
            scale_context(cx_tg, cx_t)
            dve.wait_ge(key_int_ready, 1)
            nc.vector.tensor_scalar(key_half[:], key_int[:], float(HALF), -float(HALF), ALU.is_ge,
                                    ALU.mult).then_inc(key_half_ready, 1)
            dve.wait_ge(key_half_ready, 1)
            nc.vector.tensor_tensor(key[:], key_int[:], key_half[:], ALU.add).then_inc(key_ready, 1)
            dve.wait_ge(in_index_part, 16)
            nc.vector.tensor_scalar(off_centre[:], index_part[:], -(HALF - 1) / 2, None, ALU.add).then_inc(off_centre_ready, 1)
            dve.wait_ge(off_centre_ready, 1)
            nc.vector.tensor_reduce(reach_part[:], off_centre[:], AX_X, ALU.max,
                                    apply_absolute_value=True).then_inc(reach_part_ready, 1)
            take_mean(0)
            invert_norm(rescale, 0)
            dve.wait_ge(reach_part_turned, 1)
            nc.vector.tensor_reduce(reach_max[:], ps_t[0:1, 0, 0:P], AX_X, ALU.max).then_inc(max_ready, 1)
            dve.wait_ge(max_ready, 1)
            nc.vector.tensor_scalar(beyond[:], reach_max[:], float(HALF // 2), None, ALU.is_gt).then_inc(beyond_ready, 1)
            dve.wait_ge(key_ready, 1)
            dve.wait_ge(in_index, 16)
            find(0, PAIR)
            dve.wait_ge(rescale_ready, 1)
            fill_table(table, 0, rescale, k_table, 0)

            dve.wait_ge(beyond_ready, 1)
            is_beyond = dve.value_load(beyond[0:1, 0:1], min_val=0, max_val=1)
            with dve.If(is_beyond > 0):
                dve.wait_ge(in_index_rest, 16)
                dve.wait_ge(in_index, 16)
                nc.vector.memset(far_k[:], 0.0).then_inc(far_cleared, 1)
                nc.vector.memset(far_v[:], 0.0).then_inc(far_cleared, 1)
                nc.vector.tensor_copy(far_key[:], key[:]).then_inc(far_key_ready, 1)
                dve.wait_ge(far_cleared, 2)
                dve.wait_ge(far_key_ready, 1)
                dve.wait_ge(k_table["ready"], NEIGHBOURS)
                nc.vector.memset(far_start[:], 0.0).then_inc(far_added, 1)
                with dve.Fori(1, BLOCKS) as b:
                    dve.wait_ge(far_in, b * FAR_LOADS)
                    scale_context(far_cx_tg, far_cx_t)
                    nc.vector.tensor_scalar(far_key[:], far_key[:], float(HALF), None, ALU.add).then_inc(far_key_ready, 1)
                    dve.wait_ge(far_key_ready, b + 1)
                    take_mean(b)
                    invert_norm(far_rescale, b)
                    dve.wait_ge(rescale_ready, b + 1)
                    fill_table(far_table, 0, far_rescale, k_table, b)
                    fill_table(far_table, 1, far_rescale, far_v_table, b - 1)
                    with dve.Fori(0, PAIRS) as p:
                        pair_index = index_all[:, bass.ds(p * PAIR, PAIR)]
                        nc.vector.tensor_scalar(far_alias[:], pair_index, -1.0, ALIAS + 1.0, ALU.is_equal,
                                                ALU.mult).then_inc(far_alias_ready, 1)
                        dve.wait_ge(far_alias_ready, (b - 1) * PAIRS + p + 1)
                        nc.vector.scalar_tensor_tensor(out=far_index[:], in0=pair_index, scalar=KEYS + 1.0,
                                                       in1=far_alias[:], op0=ALU.min, op1=ALU.add).then_inc(far_index_ready, 1)
                        dve.wait_ge(far_index_ready, (b - 1) * PAIRS + p + 1)
                        nc.vector.tensor_scalar(far_onehot[:], far_index[:], far_key[:, 0:1], None,
                                                ALU.is_equal).then_inc(far_onehot_ready, 1)
                        dve.wait_ge(far_picked, (b - 1) * PAIRS + p + 1)
                        for far, ps in ((far_k, ps_k), (far_v, ps_v)):
                            at = far[:, bass.ds(p, 1)].rearrange("p a g -> p (a g)")
                            nc.vector.tensor_tensor(at, at, ps[:], ALU.add).then_inc(far_added, 1)
                dve.wait_ge(far_added, 1 + 2 * PAIRS * (BLOCKS - 1))

            def join_far(p):
                with dve.If(is_beyond > 0):
                    if p <= LAST:
                        dve.wait_ge(k_picked, p + 1)
                        nc.vector.tensor_tensor(ps_k[:], ps_k[:], far_k[:, p], ALU.add).then_inc(far_k_joined, 1)
                        dve.wait_ge(far_k_joined, p + 1)
                    if p >= 2:
                        dve.wait_ge(v_picked, p - 1)
                        ps = values_bank(p - 2)
                        nc.vector.tensor_tensor(ps[:], ps[:], far_v[:, p - 2], ALU.add).then_inc(far_v_joined, 1)
                        dve.wait_ge(far_v_joined, p - 1)

            def multiply_keys(p):
                dve.wait_ge(k_picked, p + 1)
                dve.wait_ge(q_copied, p + 1)
                wait_for(dve, scored, p)
                nc.vector.tensor_tensor(prod[:].rearrange(by_pair, a=2, j=NEIGHBOURS),
                                        ps_k[:].rearrange(by_pair, a=2, j=NEIGHBOURS),
                                        q[:, p % 2].unsqueeze(2).to_broadcast([P, 2, NEIGHBOURS, D]),
                                        ALU.mult).then_inc(multiplied, 1)

            def sum_heads(p):
                dve.wait_ge(multiplied, p + 1)
                wait_for(dve, clipped, p - 1)
                nc.vector.tensor_reduce(score[:, p % 2], prod[:].rearrange("p (n d) -> p n d", d=HD), AX_X,
                                        ALU.add).then_inc(scored, 1)

            def sum_weights(p):
                dve.wait_ge(weighed, p + 1)
                nc.vector.tensor_reduce(total[:].rearrange("p (a h) -> p a h", a=2),
                                        weight[:, p % 2].rearrange("p (a j h) -> p a h j", a=2, j=NEIGHBOURS), AX_X,
                                        ALU.add).then_inc(totalled, 1)

            def bound_total(p):
                dve.wait_ge(totalled, p + 1)
                dve.wait_ge(bound_ready, 2 * p + 2)
                nc.vector.scalar_tensor_tensor(out=total_b[:].rearrange("p (a h) -> p a h", a=2),
                                               in0=bound[:, 2 * p:2 * p + 2].unsqueeze(2).to_broadcast([P, 2, HEADS]),
                                               scalar=BOUND * EPS_RMS,
                                               in1=total[:].rearrange("p (a h) -> p a h", a=2), op0=ALU.add,
                                               op1=ALU.max).then_inc(bounded, 1)

            def invert_total(p):
                dve.wait_ge(bounded, p + 1)
                wait_for(dve, normalised, p)
                nc.vector.reciprocal(inverse[:], total_b[:]).then_inc(inverted, 1)

            def normalise(p):
                dve.wait_ge(inverted, p + 1)
                wait_for(dve, v_weighed, p - 1)
                nc.vector.tensor_tensor(weight_n[:, p % 2].rearrange("p (a j h) -> p a j h", a=2, j=NEIGHBOURS),
                                        weight[:, p % 2].rearrange("p (a j h) -> p a j h", a=2, j=NEIGHBOURS),
                                        inverse[:].rearrange("p (a h) -> p a h", a=2).unsqueeze(2).to_broadcast([P, 2, NEIGHBOURS, HEADS]),
                                        ALU.mult).then_inc(normalised, 1)

            def weigh_values(p, first=0, end=2):
                dve.wait_ge(normalised, p + 1)
                dve.wait_ge(v_picked, p + 1)
                wait_for(dve, summed, p - 1)
                at, n = slice(first * ND, end * ND), (end - first) * NH // 2
                return nc.vector.tensor_tensor(wv[:, p % 2, at].rearrange("p (n d) -> p n d", d=HD),
                                               values_bank(p)[:, at].rearrange("p (n d) -> p n d", d=HD),
                                               weight_n[:, p % 2, first * NH // 2:end * NH // 2].unsqueeze(2).to_broadcast([P, n, HD]),
                                               ALU.mult)

            dve.wait_ge(in_index_rest, 16)
            find(PAIR, T)

            for p in range(PAIRS):
                join_far(p)
                multiply_keys(p)
                if p >= 1:
                    sum_weights(p - 1)
                if p == LAST:
                    weigh_values(p - 2).then_inc(v_weighed, 1)
                    bound_total(p - 1)
                    sum_heads(p)
                else:
                    sum_heads(p)
                    if p >= 1:
                        bound_total(p - 1)
                    if p >= 2:
                        weigh_values(p - 2).then_inc(v_weighed, 1)
                if p >= 1:
                    invert_total(p - 1)
            join_far(LAST + 1)
            normalise(LAST - 1)
            weigh_values(LAST - 1, 0, 1).then_inc(first_v_weighed, 1)
            sum_weights(LAST)
            weigh_values(LAST - 1, 1, 2).then_inc(v_weighed, 1)
            bound_total(LAST)
            invert_total(LAST)
            normalise(LAST)
            join_far(LAST + 2)
            for a in range(2):
                weigh_values(LAST, a, a + 1).then_inc(last_v_weighed, 1)

            w = wv[:, LAST % 2].rearrange(by_pair, a=2, j=NEIGHBOURS)
            for a in range(2):
                dve.wait_ge(last_v_weighed, a + 1)
                nc.vector.tensor_tensor(last_part[:, a], w[:, a, 0], w[:, a, 1], ALU.add).then_inc(last_half_summed, 1)
            dve.wait_ge(turned, LAST - 1)
            for a in range(2):
                dve.wait_ge(last_half_summed, a + 1)
                nc.vector.tensor_tensor(o[:, LAST % 2, a], last_part[:, a], w[:, a, 2], ALU.add).then_inc(last_summed, 1)

            before = slice(2 * LAST - 2, 2 * LAST)
            dve.wait_ge(y_ready, LAST)
            nc.vector.tensor_tensor(xs[:, before], xs[:, before], ps_qy[:], ALU.add).then_inc(last_finished, 1)
            for a in range(2):
                dve.wait_ge(last_y_ready, a + 1)
                n = 2 * LAST + a
                nc.vector.tensor_tensor(xs[:, n], xs[:, n], last_y[a], ALU.add).then_inc(last_finished, 1)

        @block.gpsimd
        def _(pool):
            nc.gpsimd.memset(zeros[:], 0.0).then_inc(zeros_ready, 1)
            nc.gpsimd.memset(ident[:], 0.0).then_inc(ident_zero, 1)
            nc.gpsimd.iota(key_int[:], [[0, 1]], base=0, channel_multiplier=1).then_inc(key_int_ready, 1)
            pool.wait_ge(ident_zero, 1)
            nc.gpsimd.affine_select(out=ident[:], in_=ident[:], compare_op=ALU.not_equal, fill=1.0, base=0,
                                    pattern=[[-1, P]], channel_multiplier=1).then_inc(ident_ready, 1)

            for j in range(NEIGHBOURS):
                at = slice(j * D, (j + 1) * D)
                pool.wait_ge(scaled_v_ready, j + 1)
                nc.gpsimd.tensor_tensor(table[HALF:P, 1, at], scaled_v[HALF:P, at],
                                        table[HALF:P, 1, at].bitcast(F32), ALU.subtract).then_inc(v_table["ready"], 1)

            def sum_neighbours(p):
                pool.wait_ge(v_weighed, p + 1)
                wait_for(pool, summed, p)
                w = wv[:, p % 2].rearrange(by_pair, a=2, j=NEIGHBOURS)
                nc.gpsimd.tensor_tensor(part[:], w[:, :, 0], w[:, :, 1], ALU.add).then_inc(half_summed, 1)
                pool.wait_ge(half_summed, p + 1)
                wait_for(pool, turned, p - 1)
                nc.gpsimd.tensor_tensor(o[:, p % 2], part[:], w[:, :, 2], ALU.add).then_inc(summed, 1)

            def normalise(p):
                pool.wait_ge(inverted, p + 1)
                wait_for(pool, v_weighed, p - 1)
                nc.gpsimd.tensor_tensor(weight_n[:, p % 2].rearrange("p (a j h) -> p a j h", a=2, j=NEIGHBOURS),
                                        weight[:, p % 2].rearrange("p (a j h) -> p a j h", a=2, j=NEIGHBOURS),
                                        inverse[:].rearrange("p (a h) -> p a h", a=2).unsqueeze(2).to_broadcast([P, 2, NEIGHBOURS, HEADS]),
                                        ALU.mult).then_inc(normalised, 1)

            def add_x(p):
                pool.wait_ge(y_copied, p + 1)
                nc.gpsimd.tensor_tensor(xs[:, 2 * p:2 * p + 2], xs[:, 2 * p:2 * p + 2], y_buffer(p),
                                        ALU.add).then_inc(finished, 1)

            pool.wait_ge(v_table["ready"], NEIGHBOURS)
            normalise(0)
            for p in range(LAST - 1):
                if p + 1 < LAST - 1:
                    normalise(p + 1)
                sum_neighbours(p)
                if 2 <= p < LAST - 2:
                    add_x(p - 2)
            w = wv[:, (LAST - 1) % 2].rearrange(by_pair, a=2, j=NEIGHBOURS)
            pool.wait_ge(first_v_weighed, 1)
            pool.wait_ge(summed, LAST - 1)
            nc.gpsimd.tensor_tensor(part[:, 0], w[:, 0, 0], w[:, 0, 1], ALU.add).then_inc(half_summed, 1)
            pool.wait_ge(half_summed, LAST)
            pool.wait_ge(turned, LAST - 2)
            nc.gpsimd.tensor_tensor(o[:, (LAST - 1) % 2, 0], part[:, 0], w[:, 0, 2], ALU.add)
            pool.wait_ge(v_weighed, LAST)
            nc.gpsimd.tensor_tensor(part[:, 1], w[:, 1, 0], w[:, 1, 1], ALU.add).then_inc(half_summed, 1)
            pool.wait_ge(half_summed, LAST + 1)
            nc.gpsimd.tensor_tensor(o[:, (LAST - 1) % 2, 1], part[:, 1], w[:, 1, 2], ALU.add).then_inc(summed, 1)
            for p in (LAST - 4, LAST - 3, LAST - 2):
                add_x(p)

        @block.tensor
        def _(pe):
            def project_context(columns, kv, steps, parts=range(NEIGHBOURS)):
                ps = (ps_k, ps_v)[kv]
                for j in parts:
                    for c in range(C):
                        rows = columns[:, c, j].rearrange("p a v -> p (a v)")
                        last = nc.tensor.matmul(ps[:, j * D:(j + 1) * D], rows, wkv[:, c, kv * D:(kv + 1) * D],
                                                start=c == 0, stop=c == C - 1)
                    if j > 0:
                        last.then_inc(steps["projected"], 1)

            def pick(ps, onehots, rows, kv):
                for a in range(2):
                    at = a * ND
                    while at < (a + 1) * ND:
                        end = min((a + 1) * ND, (at // BANK + 1) * BANK)
                        last = nc.tensor.matmul(ps[:, at:end], onehots[:, a * P:(a + 1) * P],
                                                rows[:, kv, at - a * ND:end - a * ND], start=True, stop=True)
                        at = end
                return last

            def project_q(p):
                pe.wait_ge(in_x_t[p % 2], 16 * (p // 2 + 1))
                if p == 0:
                    pe.wait_ge(wq_ready, C)
                wait_for(pe, q_copied, p)
                wait_for(pe, y_copied, p - 5)
                for a in range(2):
                    for c in range(C):
                        last = nc.tensor.matmul(ps_qy[:, a], xt[:, p % 2, c, a * P:(a + 1) * P], wq[:, c],
                                                start=c == 0, stop=c == C - 1)
                last.then_inc(q_ready, 1)

            def pick_keys(p):
                pe.wait_ge(onehot_ready, 1 if p == 0 else 2)
                wait_for(pe, multiplied, p)
                pick(ps_k, onehot[:, p * PAIR:(p + 1) * PAIR], table, 0).then_inc(k_picked, 1)

            def pick_values(p):
                if p == LAST:
                    pe.wait_ge(multiplied, PAIRS)
                else:
                    wait_for(pe, v_weighed, p)
                pick(values_bank(p), onehot[:, p * PAIR:(p + 1) * PAIR], table, 1).then_inc(v_picked, 1)

            def turn(p):
                pe.wait_ge(summed, p + 1)
                wait_for(pe, turned_copied, p)
                for a in range(2):
                    for c in range(C):
                        last = nc.tensor.transpose(ps_t[:, c, a * P:(a + 1) * P], o[:, p % 2, a, c * P:(c + 1) * P], ident[:])
                last.then_inc(turned, 1)

            def project_out_tile(p, a, to):
                for c in range(C):
                    last = nc.tensor.matmul(to, o_t[:, p % 2, c, a * P:(a + 1) * P], wo[:, c],
                                            start=c == 0, stop=c == C - 1)
                return last

            def project_out(p):
                pe.wait_ge(turned_copied, p + 1)
                pe.wait_ge(q_copied, min(p + 6, PAIRS))
                wait_for(pe, y_copied, p)
                if p == 0:
                    pe.wait_ge(in_o, 16)
                for a in range(2):
                    last = project_out_tile(p, a, ps_qy[:, a])
                last.then_inc(y_ready, 1)

            pe.wait_ge(zeros_ready, 1)
            for _ in range(WARM_UPS):
                nc.tensor.matmul(ps_v[:, 0:P], zeros[:], zeros[:], start=True, stop=True)
            pe.wait_ge(in_k, 16)
            pe.wait_ge(cx_tg_ready, C)
            project_context(cx_tg, 0, k_table, (0, 1))
            pe.wait_ge(reach_part_ready, 1)
            pe.wait_ge(ident_ready, 1)
            nc.tensor.transpose(ps_t[0:1, 0, 0:P], reach_part[:], ident[:]).then_inc(reach_part_turned, 1)
            project_context(cx_tg, 0, k_table, (2,))
            project_q(0)

            pe.wait_ge(beyond_ready, 1)
            is_beyond = pe.value_load(beyond[0:1, 0:1], min_val=0, max_val=1)
            with pe.If(is_beyond > 0):
                pe.wait_ge(in_v, 16)
                with pe.Fori(1, BLOCKS) as b:
                    pe.wait_ge(far_added, (b - 1) * (2 * PAIRS) + 1)
                    pe.wait_ge(cx_tg_ready, (b + 1) * C)
                    project_context(far_cx_tg, 0, k_table)
                    project_context(far_cx_tg, 1, far_v_table)
                    with pe.Fori(0, PAIRS) as p:
                        pe.wait_ge(far_v_table["ready"], b * NEIGHBOURS)
                        pe.wait_ge(far_onehot_ready, (b - 1) * PAIRS + p + 1)
                        pe.wait_ge(far_added, ((b - 1) * PAIRS + p) * 2 + 1)
                        pick(ps_k, far_onehot, far_table, 0)
                        pick(ps_v, far_onehot, far_table, 1).then_inc(far_picked, 1)
                pe.wait_ge(far_added, 1 + 2 * PAIRS * (BLOCKS - 1))

            pe.wait_ge(k_table["ready"], NEIGHBOURS)
            pick_keys(0)
            project_q(1)
            for p in range(LAST - 1):
                if p >= 4:
                    project_out(p - 4)
                pick_keys(p + 1)
                if p == 0:
                    pe.wait_ge(in_v, 16)
                    project_context(cx_tg, 1, v_table)
                if p >= 3:
                    turn(p - 3)
                project_q(p + 2)
                if p == 1:
                    pe.wait_ge(v_table["ready"], NEIGHBOURS)
                if p >= 1:
                    pick_values(p - 1)
            project_out(LAST - 5)
            pick_keys(LAST)
            turn(LAST - 4)
            pick_values(LAST - 2)
            project_out(LAST - 4)
            turn(LAST - 3)
            pick_values(LAST - 1)
            pick_values(LAST)
            for p in (LAST - 3, LAST - 2):
                project_out(p)
                turn(p + 1)

            def turn_last(a):
                pe.wait_ge(last_summed, a + 1)
                for c in range(C):
                    last = nc.tensor.transpose(last_t[a][:, c], o[:, LAST % 2, a, c * P:(c + 1) * P], ident[:])
                last.then_inc(last_turned, 1)

            pe.wait_ge(v_weighed, LAST)
            pe.wait_ge(turned_copied, LAST)
            pe.wait_ge(y_copied, LAST - 1)
            project_out_tile(LAST - 1, 0, ps_qy[:, 0])
            turn_last(0)
            turn_last(1)
            project_out_tile(LAST - 1, 1, ps_qy[:, 1]).then_inc(y_ready, 1)
            pe.wait_ge(last_v_weighed, 2)
            for a in range(2):
                pe.wait_ge(last_turned_copied, a + 1)
                project_out_tile(LAST, a, last_y[a]).then_inc(last_y_ready, 1)


def kernel(x, ctx_1024, itok_BxS_0_255, L0_xattn_gamma_q, L0_xattn_gamma_kv, L0_xattn_Wq, L0_xattn_Wk, L0_xattn_Wv,
           L0_xattn_Wo):
    import concourse.bacc as bacc
    from concourse.bass_utils import run_bass_kernel_spmd

    x = np.asarray(x)
    ctx = np.asarray(ctx_1024)[0]
    zeros = np.zeros((ROWS - len(ctx) - 2, ctx.shape[1]), ctx.dtype)
    ctx = np.concatenate([zeros[:1], ctx, zeros, ctx[:1]])
    index = np.asarray(itok_BxS_0_255)
    arrays = {
        "x": x[0],
        "x_t": x[0].T,
        "ctx": ctx,
        "ctx_t": np.concatenate([np.stack([np.asarray(L0_xattn_gamma_q), np.asarray(L0_xattn_gamma_kv)]), ctx]).T,
        "index_row": index,
        "index_cols": index.reshape(P, -1),
        "wq_t": np.asarray(L0_xattn_Wq).T,
        "wkv_t": np.concatenate([np.asarray(L0_xattn_Wk).T, np.asarray(L0_xattn_Wv).T], axis=1),
        "wo_t": np.asarray(L0_xattn_Wo).T,
    }
    arrays = {name: np.ascontiguousarray(a) for name, a in arrays.items()}
    nc = bacc.Bacc("TRN2", target_bir_lowering=False, num_devices=1)
    args = {n: nc.dram_tensor(n, a.shape, mybir.dt.from_np(a.dtype), kind="ExternalInput").ap()
            for n, a in arrays.items()}
    y = nc.dram_tensor("y", x[0].shape, F32, kind="ExternalOutput").ap()
    local_attention(nc, y=y, **args)
    r = run_bass_kernel_spmd(nc, [arrays], core_ids=[0])
    return r.results[0]["y"].reshape(x.shape)
```
